# Optimizing a Trainium2 kernel written in Bass

```python
import numpy as np
import jax
import jax.numpy as jnp

def _softmax(x, axis=-1):
    return jax.nn.softmax(x, axis=axis)

def _gelu(x):
    return jax.nn.gelu(x, approximate=True)

def _silu(x):
    return jax.nn.silu(x)

def _sigmoid(x):
    return jax.nn.sigmoid(x)

def _layernorm(x, axis=-1, eps=1e-05):
    m = jnp.mean(x, axis=axis, keepdims=True)
    v = jnp.var(x, axis=axis, keepdims=True)
    return (x - m) / jnp.sqrt(v + eps)

def _scatter_add(tgt, idx, src, axis=0):
    return tgt.at[idx].add(src)

def _segment_sum(src, seg, n):
    return jax.ops.segment_sum(src, seg, n)
kernel_name = 'mk_cond_resid_d1_seqx_r2_40d3d4'

def setup_inputs(seed: int=0):
    np.random.seed(seed)
    _w = jnp.asarray

    def _rec_inputs():
        import jax
        import jax.numpy as jnp
        _rk = jax.random.key(seed)
        x = -0.0002928 + 1 * jax.random.normal(jax.random.fold_in(_rk, 1), (8, 512, 512), jnp.float32)
        _lenS = 512 - jax.random.randint(jax.random.fold_in(_rk, 7), (8,), 0, max(1, 512 // 4) + 1, jnp.int32)
        _lenS2 = 512 - jax.random.randint(jax.random.fold_in(_rk, 8), (8,), 0, max(1, 512 // 4) + 1, jnp.int32)
        fside_16xSxS_0 = -5.72187e-05 + 0.999849 * jax.random.normal(jax.random.fold_in(_rk, 11), (16, 512, 512), jnp.float32)
        cond_64 = -0.0265395 + 0.99382 * jax.random.normal(jax.random.fold_in(_rk, 13), (8, 64), jnp.float32)
        _validS = jnp.arange(512)[None, :] < _lenS[:, None]
        _validS2 = jnp.arange(512)[None, :] < _lenS2[:, None]
        _causal = jnp.tril(jnp.ones((512, 512), dtype=bool))
        mask_BxS_bk0 = jnp.logical_not(jnp.broadcast_to(_validS[:, :], (8, 512)))
        return (x, fside_16xSxS_0, cond_64, mask_BxS_bk0)
    x, fside_16xSxS_0, cond_64, mask_BxS_bk0 = _rec_inputs()

    def _L0_cond_setup():
        import jax, jax.numpy as jnp
        import numpy as np
        B, N, DIM, H, DH = (2, 1024, 512, 16, 64)
        INNER = H * DH
        EPS = 1e-05

        def layernorm(x, g):
            mean = jnp.mean(x, axis=-1, keepdims=True)
            var = jnp.var(x, axis=-1, keepdims=True)
            return (x - mean) * jax.lax.rsqrt(var + EPS) * g
        key = jax.random.key(seed)
        ks = jax.random.split(key, 10)
        x = jax.random.normal(ks[0], (B, N, DIM), dtype=jnp.float32)
        attn_bias = jax.random.normal(ks[1], (H, N, N), dtype=jnp.float32)
        mask = jax.random.randint(ks[2], (B, N), 0, 2).astype(bool)
        g_in = jnp.ones((DIM,), dtype=jnp.float32)
        null_attn_bias = jax.random.normal(ks[3], (H,), dtype=jnp.float32)
        null_kv = jax.random.normal(ks[4], (2, DH), dtype=jnp.float32)
        Wq = jax.random.normal(ks[5], (DIM, INNER), dtype=jnp.float32) * 0.02
        Wkv = jax.random.normal(ks[6], (DIM, 2 * DH), dtype=jnp.float32) * 0.02
        Wo = jax.random.normal(ks[7], (INNER, DIM), dtype=jnp.float32) * 0.02
        g_out = jnp.ones((DIM,), dtype=jnp.float32)
        return {'x': x, 'attn_bias': attn_bias, 'mask': mask, 'g_in': g_in, 'null_attn_bias': null_attn_bias, 'null_kv': null_kv, 'Wq': Wq, 'Wkv': Wkv, 'Wo': Wo, 'g_out': g_out}
    _L0_cond_all = _L0_cond_setup()
    _L0_cond_in = {k: v for k, v in _L0_cond_all.items() if k in ('g_in', 'null_attn_bias', 'Wq', 'Wkv', 'Wo', 'g_out')}
    del _L0_cond_all
    return {'x': x, 'fside_16xSxS_0': fside_16xSxS_0, 'cond_64': cond_64, 'mask_BxS_bk0': mask_BxS_bk0, 'L0_cond_g_in': _L0_cond_in['g_in'], 'L0_cond_null_attn_bias': _L0_cond_in['null_attn_bias'], 'L0_cond_Wq': _L0_cond_in['Wq'], 'L0_cond_Wkv': _L0_cond_in['Wkv'], 'L0_cond_Wo': _L0_cond_in['Wo'], 'L0_cond_g_out': _L0_cond_in['g_out']}

def reference(x, fside_16xSxS_0, cond_64, mask_BxS_bk0, L0_cond_g_in, L0_cond_null_attn_bias, L0_cond_Wq, L0_cond_Wkv, L0_cond_Wo, L0_cond_g_out):
    import jax
    import jax.numpy as jnp

    def _L0_cond_ref(x, attn_bias, mask, g_in, null_attn_bias, null_kv, Wq, Wkv, Wo, g_out):
        import jax, jax.numpy as jnp
        import numpy as np
        B, N, DIM, H, DH = (2, 1024, 512, 16, 64)
        INNER = H * DH
        EPS = 1e-05

        def layernorm(x, g):
            mean = jnp.mean(x, axis=-1, keepdims=True)
            var = jnp.var(x, axis=-1, keepdims=True)
            return (x - mean) * jax.lax.rsqrt(var + EPS) * g
        b, n, _ = x.shape
        scale = DH ** (-0.5)
        xn = layernorm(x, g_in)
        q = (xn @ Wq).reshape(b, n, H, DH).transpose(0, 2, 1, 3) * scale
        kv = xn @ Wkv
        k, v = (kv[..., :DH], kv[..., DH:])
        nk = jnp.broadcast_to(null_kv[0], (b, 1, DH))
        nv = jnp.broadcast_to(null_kv[1], (b, 1, DH))
        k = jnp.concatenate([nk, k], axis=1)
        v = jnp.concatenate([nv, v], axis=1)
        sim = jnp.einsum('bhid,bjd->bhij', q, k)
        null_col = jnp.broadcast_to(null_attn_bias[:, None, None], (H, n, 1))
        bias = jnp.concatenate([null_col, attn_bias], axis=-1)
        sim = sim + bias
        neg = -jnp.finfo(sim.dtype).max
        j = n + 1
        causal_mask = jnp.triu(jnp.ones((n, j), dtype=bool), k=j - n + 1)
        sim = jnp.where(causal_mask, neg, sim)
        mask_p = jnp.pad(mask, ((0, 0), (1, 0)), constant_values=True)
        sim = jnp.where(mask_p[:, None, None, :], sim, neg)
        attn = jax.nn.softmax(sim, axis=-1)
        out = jnp.einsum('bhij,bjd->bhid', attn, v)
        out = out.transpose(0, 2, 1, 3).reshape(b, n, INNER)
        out = out @ Wo
        return layernorm(out, g_out)
    x = x + _L0_cond_ref(x, fside_16xSxS_0, mask_BxS_bk0, L0_cond_g_in, L0_cond_null_attn_bias, cond_64, L0_cond_Wq, L0_cond_Wkv, L0_cond_Wo, L0_cond_g_out)
    return x

_drawn_inputs = setup_inputs


def setup_inputs(seed=0):
    import zlib

    import numpy as np

    out = dict(_drawn_inputs(seed))
    spreads = {'L0_cond_g_in': (1.0, 0.2), 'L0_cond_g_out': (1.0, 0.2)}
    factors = {}
    for name, (base, spread) in spreads.items():
        noise = np.random.default_rng([zlib.crc32(name.encode()), seed]).standard_normal(out[name].shape)
        drawn = base * np.exp(spread * noise) if base else spread * noise
        out[name] = jnp.asarray(drawn.astype(out[name].dtype))
    for name, factor in factors.items():
        out[name] = (out[name] * factor).astype(out[name].dtype)
    return out
```

```python
from contextlib import ExitStack

import concourse.bass as bass
import numpy as np
from concourse import mybir

F32 = mybir.dt.float32
BF16 = mybir.dt.bfloat16
I32 = mybir.dt.int32
U8 = mybir.dt.uint8
ALU = mybir.AluOpType
ACT = mybir.ActivationFunctionType
AX = mybir.AxisListType

P = 128
B, S, D, H, DH = 8, 512, 512, 16, 64
INNER = H * DH
EPS = 1e-5
SCALE = DH ** -0.5
NEG = -1e30
ROOT_GAIN = -8192.0
ROOT_STEPS = 9
NB = S // P
KT = D // P
CT = INNER // P
UNITS = B * NB
ITEMS = B * NB * (NB + 1) // 2
G = 4
HG = H // G
GW = HG * P
BANK = 512
IB = 4

T_ROWS, T_KV, T_SLOT, T_BIAS, T_OFF = range(5)
T_BEGUN, T_ENDED, T_LOADS = range(3)


def constants():
    e = np.arange(NB * B * NB)
    i, b, j = e // (B * NB), e // NB % B, e % NB
    upto = e[:, None] <= e[None, :]
    same_unit = (i[:, None] == i[None, :]) & (b[:, None] == b[None, :])
    same_bias = (i[:, None] == i[None, :]) & (j[:, None] == j[None, :])
    r = np.arange(UNITS)
    tri32 = np.zeros((P, UNITS))
    tri32[:UNITS] = r[:, None] <= r[None, :]

    def steps(values):
        return np.append(values[1:], 0) - values

    lists = np.stack([steps(b * NB + i), steps(b * NB + j), steps(j), steps(i * NB + j), steps((i != j) * 1)], 1)
    q = np.arange(P)
    parts = {
        "causal": (j <= i)[:, None],
        "upto": upto,
        "upto_unit": upto & same_unit,
        "from_unit": upto.T & same_unit,
        "upto_bias": upto & same_bias,
        "of_unit": (b * NB + i)[:, None] == r[None, :],
        "upto_rows": tri32,
        "iota": np.tile(np.arange(P), (P, 1)),
        "lists": lists,
        "ident": np.eye(P),
        "tri": np.concatenate([np.where(q[None, :] > q[:, None], NEG, 0.0), np.zeros((P, P))], 1),
    }
    return {k: np.asarray(v, np.float32) for k, v in parts.items()}


def attention(nc, x, bias, keep, keep_row, cond, g_in, null_bias, wq, wkv, wo, g_out, const, out):
    parts = constants()
    where, at = {}, 0
    for name, a in parts.items():
        where[name] = (at, at + a.shape[1])
        at += a.shape[1]
    width = at

    with ExitStack() as ctx:
        def sb(name, shape, dt=F32):
            return ctx.enter_context(nc.sbuf_tensor(name, shape, dt))

        def sem(name):
            return ctx.enter_context(nc.semaphore(name))

        const_sb = sb("const_sb", [P, width])

        def c(name, rows=P):
            a, z = where[name]
            return const_sb[0:rows, a:z]

        ident = c("ident")
        ident_b = sb("ident_b", [P, P], BF16)
        ones = sb("ones", [P, H])
        wq_sb = sb("wq_sb", [P, KT, INNER])
        wkk_sb = sb("wkk_sb", [P, KT, P])
        wvn_sb = sb("wvn_sb", [P, KT, DH + H])
        wo_sb = sb("wo_sb", [P, CT, D])
        gin_sb = sb("gin_sb", [P, KT])
        ginq_sb = sb("ginq_sb", [P, KT])
        gink_sb = sb("gink_sb", [P, KT])
        gout_sb = sb("gout_sb", [P, D])
        nkey_sb = sb("nkey_sb", [P, DH])
        nval_sb = sb("nval_sb", [P, DH])
        nvcol_sb = sb("nvcol_sb", [P, 1])
        nvcols_sb = sb("nvcols_sb", [P, P])
        nbias_sb = sb("nbias_sb", [P, H])
        wnull_tmp = sb("wnull_tmp", [P, INNER])
        maskadd = sb("maskadd", [P, UNITS * P], BF16)
        keep_bc = sb("keep_bc", [P, UNITS * P], U8)
        null_row = sb("null_row", [P, D])

        keep_e = sb("keep_e", [P, P], U8)
        active = sb("active", [P, 1])
        counts = sb("counts", [P, 4])
        flags = sb("flags", [P, 3])
        le0 = sb("le0", [P, P])
        le1 = sb("le1", [P, P])
        idle = sb("idle", [UNITS, 1])
        idle_upto = sb("idle_upto", [UNITS, 1])
        le_idle = sb("le_idle", [UNITS, UNITS])
        tab = sb("tab", [5, P], I32)
        tab_n = sb("tab_n", [3, P + 1], I32)
        tab_run = sb("tab_run", [1, P], I32)
        tab_idle = sb("tab_idle", [1, UNITS + 2 * IB], I32)
        total = sb("total", [1, 2], I32)

        x_sb = sb("x_sb", [P, 2 * D])
        x_stats = sb("x_stats", [P, 6])
        x_mv = sb("x_mv", [P, 2])
        x_rstd = sb("x_rstd", [P, 1])
        x_var = sb("x_var", [P, 1])
        x_t = sb("x_t", [P, 1])
        xn = sb("xn", [P, D])
        xT = sb("xT", [P, KT, P])
        qT = sb("qT", [P, CT, P])
        k_store = sb("k_store", [P, UNITS * P])
        v_store = sb("v_store", [P, UNITS * DH])
        bias_sb = sb("bias_sb", [P, NB * H * P])

        null_raw = sb("null_raw", [P, H])

        k_cur = sb("k_cur", [P, P])
        v_cur = sb("v_cur", [P, DH])
        mask_cur = sb("mask_cur", [P, P], BF16)
        s_sb = sb("s_sb", [P, H, P])
        p_T = sb("p_T", [P, 2, GW])
        m_grp = sb("m_grp", [P, H])
        m_new = sb("m_new", [P, H])
        m_neg = sb("m_neg", [P, H])
        m_drop = sb("m_drop", [P, H])
        alpha = sb("alpha", [P, H])
        p_sum = sb("p_sum", [P, H])
        l_old = sb("l_old", [P, H])
        m_st = sb("m_st", [P, 2 * H])
        l_st = sb("l_st", [P, 2 * H])
        o_st = sb("o_st", [P, 2 * INNER])

        l_inv = sb("l_inv", [P, H])
        o_n = sb("o_n", [P, INNER])
        o_T = sb("o_T", [P, CT, P])
        y_stats = sb("y_stats", [P, 6])
        y_mv = sb("y_mv", [P, 2])
        y_rstd = sb("y_rstd", [P, 1])
        y_var = sb("y_var", [P, 1])
        y_t = sb("y_t", [P, 1])
        y_sb = sb("y_sb", [P, D])

        idle_sb = sb("idle_sb", [P, IB, D])

        ps = ctx.enter_context(nc.psum_tensor("ps", [P, 8, BANK], F32))
        ps_q = (0, 1)
        ps_x = 2
        ps_kv = 3
        ps_s = (4, 5)
        ps_t = (6, 7)

        s_const, s_keep, s_wq, s_wkv, s_wo, s_small, s_keepbc = (
            sem(n) for n in ("const_in", "keep_in", "wq_in", "wkv_in", "wo_in", "small_in", "keepbc_in"))
        s_tabv, s_tabp, s_tab = sem("tab_dve"), sem("tab_pe"), sem("tab_ready")
        s_ones, s_identb, s_wqs, s_wks, s_wn, s_prep = (
            sem(n) for n in ("ones_ready", "identb_ready", "wq_scaled", "wkv_scaled", "wnull", "dve_prep"))
        s_init, s_maskadd = sem("state_init"), sem("maskadd_ready")
        s_nvcols, s_null_ps, s_nullv, s_null = (
            sem(n) for n in ("nvcols_ready", "null_ps", "null_dve", "null_row_ready"))
        s_alone = sem("waited_alone")
        s_nroot = sem("null_root")
        s_x, s_xstat, s_xmv, s_xrstd, s_xn = (sem(n) for n in ("x_in", "x_stats", "x_mv", "x_rstd", "xn_ready"))
        s_xT_ps = sem("xT_ps")
        s_xT, s_q_ps, s_q, s_kv_ps = (sem(n) for n in ("xT_ready", "q_ps", "qT_ready", "kv_ps"))
        s_kv = sem("kv_ready")
        s_m0 = sem("m0_ready")
        s_kcur, s_vcur, s_mcur, s_bias = (sem(n) for n in ("kcur", "vcur", "maskcur", "bias_in"))
        s_s_ps = sem("scores_ps")
        s_add = sem("scores_added")
        s_mgrp, s_mnew, s_mneg = (sem(n) for n in ("m_grp", "m_new", "m_neg"))
        s_alpha, s_p = sem("alpha_ready"), sem("p_ready")
        s_pt_ps = sem("pT_ps")
        s_pt = sem("pT_ready")
        s_pv = sem("pv_ps")
        s_lold, s_l, s_omul = sem("l_old"), sem("l_ready"), sem("o_scaled")
        s_o = sem("o_added")
        s_linv, s_on = sem("l_inv"), sem("o_norm")
        s_ot_ps = sem("oT_ps")
        s_ot = sem("oT_ready")
        s_y_ps, s_ystat, s_ymv, s_yrstd = (sem(n) for n in ("y_ps", "y_stats", "y_mv", "y_rstd"))
        s_yread = sem("y_read")
        s_yg = sem("y_gained")
        s_y = sem("y_ready")
        s_yout = sem("y_out")
        s_idle_in = [sem(f"idle_in{k}") for k in range(IB)]
        s_idle_out = [sem(f"idle_out{k}") for k in range(IB)]
        s_idle = sem("idle_added")

        x_rows = x.rearrange("b s d -> (b s) d")
        out_rows = out.rearrange("b s d -> (b s) d")
        block = ctx.enter_context(nc.Block())

        def row(eng, table, r, t, high, low=0):
            return eng.value_load(table[r:r + 1, bass.ds(t, 1)], min_val=low, max_val=high)

        def wait_alone(eng, semaphore, value):
            eng.wait_ge(semaphore, value)
            eng.sem_inc(s_alone, 1)

        def begun(eng, t):
            return (row(eng, tab_n, T_BEGUN, t + 1, UNITS, 1), row(eng, tab_n, T_BEGUN, t + 2, UNITS, 1))

        @block.sync
        def _(sp):
            sp.sem_inc(s_yout, 16)
            for k in range(NB):
                sp.dma_start(keep_e[k * UNITS:(k + 1) * UNITS, :], keep).then_inc(s_keep, 16)
            sp.dma_start(const_sb[:, :], const).then_inc(s_const, 16)
            sp.dma_start(wq_sb[:, :, :], wq.rearrange("(t p) n -> p t n", p=P)).then_inc(s_wq, 16)
            sp.dma_start(wo_sb[:, :, :], wo.rearrange("(t p) n -> p t n", p=P)).then_inc(s_wo, 16)
            sp.wait_ge(s_tab, 6)
            n_items = sp.value_load(total[0:1, 0:1], min_val=0, max_val=ITEMS)

            def load_x(n1, t):
                r = row(sp, tab, T_ROWS, t, UNITS - 1)
                sp.dma_start(x_sb[:, bass.ds((n1 % 2) * D, D)], x_rows[bass.ds(r * P, P), :]).then_inc(s_x, 16)

            with sp.If(n_items > 0):
                load_x(1, 0)
                with sp.Fori(0, ITEMS) as t:
                    with sp.If(t < n_items):
                        n, nn = begun(sp, t)
                        ended = row(sp, tab_n, T_ENDED, t + 1, UNITS)
                        l0 = row(sp, tab_n, T_LOADS, t, UNITS)
                        l1 = row(sp, tab_n, T_LOADS, t + 1, UNITS)
                        with sp.If(l1 > l0):
                            slot = row(sp, tab, T_SLOT, t, NB - 1)
                            tile = row(sp, tab, T_BIAS, t, NB * NB - 1)
                            wait_alone(sp, s_add, G * (t + 1))
                            sp.dma_start(bias_sb[:, bass.ds(slot * (H * P), H * P)],
                                         bias[bass.ds(tile * P, P), :]).then_inc(s_bias, 16)
                        with sp.If(nn > n):
                            n_next = sp.snap(nn, min_val=2)
                            wait_alone(sp, s_y, n_next)
                            wait_alone(sp, s_x, 16 * n)
                            load_x(n_next, t + 1)
                        with sp.If(ended == n):
                            r = row(sp, tab, T_ROWS, t, UNITS - 1)
                            wait_alone(sp, s_y, n + 2)
                            sp.dma_start(out_rows[bass.ds(r * P, P), :], y_sb[:, :]).then_inc(s_yout, 16)
                        sp.nop()
                sp.nop()
            n_begun = row(sp, tab_n, T_BEGUN, ITEMS, UNITS)
            wait_alone(sp, s_yout, 16 * (n_begun + 1))
            sp.nop()

        @block.gpsimd
        def _(pool):
            pool.wait_ge(s_tab, 6)
            n_idle = pool.value_load(total[0:1, 1:2], min_val=0, max_val=UNITS)

            def load(s, k):
                r = row(pool, tab_idle, 0, s, UNITS - 1)
                pool.dma_start(idle_sb[:, k, :], x_rows[bass.ds(r * P, P), :]).then_inc(s_idle_in[k], 16)

            for k in range(IB):
                with pool.If(n_idle > k):
                    load(k, k)
                    pool.nop()
            with pool.Fori(0, UNITS, IB) as s0:
                for k in range(IB):
                    with pool.If(s0 + k < n_idle):
                        r = row(pool, tab_idle, 0, s0 + k, UNITS - 1)
                        pool.wait_ge(s_null, 1)
                        pool.wait_ge(s_idle_in[k], 16 * (s0 // IB + 1))
                        pool.tensor_tensor(idle_sb[:, k, :], idle_sb[:, k, :], null_row[:, :],
                                           ALU.add).then_inc(s_idle, 1)
                        wait_alone(pool, s_idle, s0 + (k + 1))
                        pool.dma_start(out_rows[bass.ds(r * P, P), :], idle_sb[:, k, :]).then_inc(s_idle_out[k], 16)
                for k in range(IB):
                    with pool.If(s0 + k + IB < n_idle):
                        wait_alone(pool, s_idle_out[k], 16 * (s0 // IB + 1))
                        load(s0 + k + IB, k)
                        pool.nop()
            for k in range(IB):
                with pool.If(n_idle > k):
                    wait_alone(pool, s_idle_out[k], 16 * ((n_idle + (IB - 1 - k)) // IB))
                    pool.nop()
            pool.nop()

        @block.tensor
        def _(pe):
            mm, tr = pe.matmul, pe.transpose
            pe.sem_inc(s_xT_ps, 1)
            pe.sem_inc(s_q_ps, 2)
            pe.sem_inc(s_s_ps, G)
            pe.sem_inc(s_pt_ps, G)
            pe.sem_inc(s_pv, G)
            pe.sem_inc(s_ot_ps, 2)

            pe.wait_ge(s_const, 16)
            pe.wait_ge(s_ones, 1)
            pe.wait_ge(s_tabv, 2)
            for k, name in enumerate(("upto", "upto_unit", "from_unit", "upto_bias")):
                mm(ps[:, 0, k:k + 1], c(name), active[:, :], start=True, stop=True)
            mm(ps[0:UNITS, 0, 4:5], c("of_unit"), active[:, :], start=True, stop=True)
            mm(ps[0:1, 0, 5:6], active[:, :], ones[:, 0:1], start=True, stop=True).then_inc(s_tabp, 1)
            pe.wait_ge(s_tabv, 7)
            mm(ps[0:5, 1, 0:P], c("lists"), le0[:, :], start=True, stop=True)
            mm(ps[0:3, 2, 0:P], flags[:, :], le1[:, :], start=True, stop=True)
            mm(ps[0:UNITS, 3, 0:1], c("upto_rows", UNITS), idle[:, :], start=True, stop=True)
            mm(ps[0:1, 3, 2:3], idle[:, :], ones[0:UNITS, 0:1], start=True, stop=True).then_inc(s_tabp, 1)
            pe.wait_ge(s_tabv, 8)
            mm(ps[0:1, 4, 0:UNITS], ones[0:UNITS, 0:1], le_idle[:, :], start=True, stop=True).then_inc(s_tabp, 1)
            pe.wait_ge(s_tab, 6)
            n_items = pe.value_load(total[0:1, 0:1], min_val=0, max_val=ITEMS)

            def prepare(n1):
                pe.wait_ge(s_xn, n1)
                for k in range(KT):
                    ins = tr(ps[:, ps_x, k * P:(k + 1) * P], xn[:, k * P:(k + 1) * P], ident)
                ins.then_inc(s_xT_ps, 1)
                pe.wait_ge(s_xT, n1)
                for a in range(CT):
                    for k in range(KT):
                        ins = mm(ps[:, ps_q[a // G], (a % G) * P:(a % G + 1) * P], wq_sb[:, k, a * P:(a + 1) * P],
                                 xT[:, k, :], start=(k == 0), stop=(k == KT - 1))
                    if a % G == G - 1:
                        ins.then_inc(s_q_ps, 1)
                pe.wait_ge(s_kv, 3 * n1)
                for k in range(KT):
                    mm(ps[:, ps_kv, 0:P], wkk_sb[:, k, :], xT[:, k, :], start=(k == 0), stop=(k == KT - 1))
                for k in range(KT):
                    ins = mm(ps[:, ps_kv, P:P + DH + H], xT[:, k, :], wvn_sb[:, k, :],
                             start=(k == 0), stop=(k == KT - 1))
                ins.then_inc(s_kv_ps, 1)

            pe.wait_ge(s_wqs, KT)
            pe.wait_ge(s_wks, KT)
            pe.wait_ge(s_wn, KT + 1)
            pe.wait_ge(s_identb, 1)
            with pe.If(n_items > 0):
                prepare(1)
                pe.nop()

            pe.wait_ge(s_wo, 16)
            pe.wait_ge(s_nvcols, 1)
            for a in range(CT):
                ins = mm(ps[:, ps_s[0], :], nvcols_sb[:, :], wo_sb[:, a, :], start=(a == 0), stop=(a == CT - 1))
            ins.then_inc(s_null_ps, 1)
            pe.wait_ge(s_nullv, 3)

            with pe.Fori(0, ITEMS) as t:
                with pe.If(t < n_items):
                    n, nn = begun(pe, t)
                    ended0 = row(pe, tab_n, T_ENDED, t, UNITS)
                    ended = row(pe, tab_n, T_ENDED, t + 1, UNITS)
                    pe.wait_ge(s_q, 2 * n)
                    pe.wait_ge(s_kcur, t + 1)
                    pe.wait_ge(s_mcur, t + 1)
                    for g in range(G):
                        half = slice((g % 2) * DH, (g % 2 + 1) * DH)
                        pe.wait_ge(s_add, G * (t + 1) + g - 1)
                        mm(ps[:, ps_s[g % 2], :], ident_b[:, :],
                           mask_cur[:, :].unsqueeze(1).to_broadcast([P, HG, P]), start=True, stop=False)
                        for k in range(HG):
                            ins = mm(ps[:, ps_s[g % 2], k * P:(k + 1) * P], qT[half, g // 2 * G + k, :],
                                     k_cur[half, :], start=False, stop=(k == HG - 1))
                        ins.then_inc(s_s_ps, 1)
                    with pe.If(nn > n):
                        n_next = pe.snap(nn, min_val=2)
                        pe.wait_ge(s_yread, n_next)
                        pe.wait_ge(s_o, 2 * (t + 1))
                        prepare(n_next)
                        pe.nop()
                    pe.wait_ge(s_ot, 2 * (ended0 + 1))
                    pe.wait_ge(s_vcur, t + 1)
                    pe.wait_ge(s_q, 2 * nn)
                    pe.wait_ge(s_o, 2 * (t + 1))
                    for g in range(G + 1):
                        if g < G:
                            pe.wait_ge(s_p, G * t + g + 1)
                            pe.wait_ge(s_pt, G * (t + 1) + g - 1)
                            for k in range(HG):
                                ins = tr(ps[:, ps_t[g % 2], k * P:(k + 1) * P], s_sb[:, g * HG + k, :], ident)
                            ins.then_inc(s_pt_ps, 1)
                        if g > 0:
                            pe.wait_ge(s_pt, G * (t + 1) + g)
                            for k in range(HG):
                                p = (g - 1) * HG + k
                                ins = mm(ps[:, ps_q[p // 8], (p % 8) * DH:(p % 8 + 1) * DH],
                                         p_T[:, (g - 1) % 2, k * P:(k + 1) * P], v_cur[:, :], start=True, stop=True)
                            ins.then_inc(s_pv, 1)
                    with pe.If(ended == n):
                        pe.wait_ge(s_on, n)
                        for a in range(CT):
                            ins = tr(ps[:, ps_t[a // G], (a % G) * P:(a % G + 1) * P], o_n[:, a * P:(a + 1) * P], ident)
                            if a % G == G - 1:
                                ins.then_inc(s_ot_ps, 1)
                        pe.wait_ge(s_xT, nn)
                        for a in range(CT):
                            if a % G == 0:
                                pe.wait_ge(s_ot, 2 * n + a // G + 1)
                            ins = mm(ps[:, ps_x, :], o_T[:, a, :], wo_sb[:, a, :], start=(a == 0), stop=(a == CT - 1))
                        ins.then_inc(s_y_ps, 1)
                        pe.nop()
                    pe.nop()

        @block.scalar
        def _(act):
            act.sem_inc(s_kv, 3)
            act.sem_inc(s_ot, 2)
            wkv_rows = wkv.rearrange("(t p) n -> p t n", p=P)
            for half in range(2):
                act.dma_start(wkk_sb[:, :, half * DH:(half + 1) * DH], wkv_rows[:, :, 0:DH]).then_inc(s_wkv, 16)
            act.dma_start(wvn_sb[:, :, 0:DH], wkv_rows[:, :, DH:2 * DH]).then_inc(s_wkv, 16)
            act.dma_start(gin_sb[:, :], g_in).then_inc(s_small, 16)
            act.dma_start(nkey_sb[:, :], cond[0:1, :].partition_broadcast(P)).then_inc(s_small, 16)
            act.dma_start(nval_sb[:, :], cond[1:2, :].partition_broadcast(P)).then_inc(s_small, 16)
            for half in range(2):
                act.dma_start(nvcol_sb[half * DH:(half + 1) * DH, :],
                              cond[1:2, :].rearrange("a d -> d a")).then_inc(s_small, 16)
            act.dma_start(nbias_sb[:, :], null_bias.partition_broadcast(P)).then_inc(s_small, 16)
            act.dma_start(gout_sb[:, :], g_out.partition_broadcast(P)).then_inc(s_small, 16)
            act.dma_start(keep_bc[:, :], keep_row.partition_broadcast(P)).then_inc(s_keepbc, 16)

            act.wait_ge(s_small, 7 * 16)
            act.mul(ginq_sb[:, :], gin_sb[:, :], SCALE / ROOT_GAIN).then_inc(s_prep, 1)
            act.mul(gink_sb[:, :], gin_sb[:, :], 1 / ROOT_GAIN).then_inc(s_prep, 1)
            act.mul(gout_sb[:, :], gout_sb[:, :], 1 / ROOT_GAIN).then_inc(s_prep, 1)
            act.wait_ge(s_prep, 2)
            act.wait_ge(s_wkv, 3 * 16)
            for k in range(KT):
                act.mul(wkk_sb[:, k, :], wkk_sb[:, k, :], gink_sb[:, k:k + 1])
                act.mul(wvn_sb[:, k, 0:DH], wvn_sb[:, k, 0:DH], gink_sb[:, k:k + 1]).then_inc(s_wks, 1)
            act.wait_ge(s_wq, 16)
            for k in range(KT):
                act.mul(wq_sb[:, k, :], wq_sb[:, k, :], ginq_sb[:, k:k + 1]).then_inc(s_wqs, 1)
            act.wait_ge(s_tab, 6)
            n_items = act.value_load(total[0:1, 0:1], min_val=0, max_val=ITEMS)

            def take_xT(n1):
                act.wait_ge(s_xT_ps, n1 + 1)
                act.copy(xT[:, :, :].rearrange("p t n -> p (t n)"), ps[:, ps_x, :]).then_inc(s_xT, 1)

            def take_qkv(n1, t):
                for a in range(2):
                    act.wait_ge(s_q_ps, 2 * n1 + 1 + a)
                    act.copy(qT[:, a * G:(a + 1) * G, :].rearrange("p t n -> p (t n)"), ps[:, ps_q[a], :]).then_inc(s_q, 1)
                r = row(act, tab, T_ROWS, t, UNITS - 1)
                act.wait_ge(s_kv_ps, n1)
                act.copy(k_store[:, bass.ds(r * P, P)], ps[:, ps_kv, 0:P]).then_inc(s_kv, 1)
                act.copy(v_store[:, bass.ds(r * DH, DH)], ps[:, ps_kv, P:P + DH]).then_inc(s_kv, 1)
                act.wait_ge(s_m0, n1)
                act.copy(null_raw[:, :], ps[:, ps_kv, P + DH:P + DH + H]).then_inc(s_kv, 1)

            with act.If(n_items > 0):
                take_xT(1)
                take_qkv(1, 0)
                act.nop()
            with act.Fori(0, ITEMS) as t:
                with act.If(t < n_items):
                    n, nn = begun(act, t)
                    ended = row(act, tab_n, T_ENDED, t + 1, UNITS)
                    kv = row(act, tab, T_KV, t, UNITS - 1)
                    act.wait_ge(s_kv, 3 * (n + 1))
                    act.wait_ge(s_s_ps, G * (t + 1))
                    act.copy(k_cur[:, :], k_store[:, bass.ds(kv * P, P)]).then_inc(s_kcur, 1)
                    act.wait_ge(s_pv, G * (t + 1))
                    act.copy(v_cur[:, :], v_store[:, bass.ds(kv * DH, DH)]).then_inc(s_vcur, 1)
                    with act.If(nn > n):
                        n_next = act.snap(nn, min_val=2)
                        take_xT(n_next)
                        act.nop()
                    act.wait_ge(s_mneg, 2 * (t + 1))
                    act.activation(alpha[:, :], m_drop[:, :], ACT.Exp).then_inc(s_alpha, 1)
                    for p in range(H):
                        ins = act.activation(s_sb[:, p, :], s_sb[:, p, :], ACT.Exp, bias=m_neg[:, p:p + 1],
                                             accum_out=p_sum[:, p:p + 1])
                        if p % HG == HG - 1:
                            ins.then_inc(s_p, 1)
                    with act.If(nn > n):
                        n_next = act.snap(nn, min_val=2)
                        take_qkv(n_next, t + 1)
                        act.nop()
                    with act.If(ended == n):
                        for a in range(2):
                            act.wait_ge(s_ot_ps, 2 * n + a + 1)
                            act.copy(o_T[:, a * G:(a + 1) * G, :].rearrange("p t n -> p (t n)"),
                                     ps[:, ps_t[a], :]).then_inc(s_ot, 1)
                        act.nop()
                    act.nop()

        @block.vector
        def _(dve):
            tt, ts = dve.tensor_tensor, dve.tensor_scalar
            dve.sem_inc(s_m0, 1)
            dve.sem_inc(s_add, G)
            dve.sem_inc(s_pt, G)
            dve.sem_inc(s_o, 2)
            dve.sem_inc(s_yread, 2)
            dve.sem_inc(s_y, 2)
            for done in (s_xrstd, s_nroot, s_yrstd):
                dve.sem_inc(done, ROOT_STEPS)
            dve.memset(ones[:, :], 1.0).then_inc(s_ones, 1)
            dve.memset(tab_n[:, 0:1], 0)
            dve.memset(l_st[:, 0:H], 1.0).then_inc(s_init, 1)

            dve.wait_ge(s_keep, NB * 16)
            dve.tensor_reduce(active[:, :], keep_e[:, :], AX.X, ALU.max).then_inc(s_tabv, 1)
            dve.wait_ge(s_const, 16)
            dve.wait_ge(s_tabv, 1)
            tt(active[:, :], active[:, :], c("causal"), ALU.mult).then_inc(s_tabv, 1)
            dve.tensor_copy(ident_b[:, :], ident).then_inc(s_identb, 1)
            dve.wait_ge(s_tabp, 1)
            dve.tensor_copy(counts[:, :], ps[:, 0, 0:4]).then_inc(s_tabv, 1)
            ts(idle[:, :], ps[0:UNITS, 0, 4:5], 0.5, None, ALU.is_lt).then_inc(s_tabv, 1)
            dve.tensor_copy(total[0:1, 0:1], ps[0:1, 0, 5:6]).then_inc(s_tab, 1)
            dve.wait_ge(s_tabv, 4)
            ts(le0[:, :], c("iota"), counts[:, 0:1], None, ALU.is_ge).then_inc(s_tabv, 1)
            ts(le1[:, :], c("iota"), 1.0, counts[:, 0:1], ALU.add, ALU.is_ge).then_inc(s_tabv, 1)
            ts(flags[:, :], counts[:, 1:4], 1.0, active[:, 0:1], ALU.is_equal, ALU.mult).then_inc(s_tabv, 1)
            dve.wait_ge(s_tabp, 2)
            dve.tensor_copy(idle_upto[:, :], ps[0:UNITS, 3, 0:1]).then_inc(s_init, 1)
            dve.tensor_copy(tab[:, :], ps[0:5, 1, 0:P]).then_inc(s_tab, 1)
            dve.tensor_copy(tab_n[:, 1:P + 1], ps[0:3, 2, 0:P]).then_inc(s_tab, 1)
            dve.tensor_copy(total[0:1, 1:2], ps[0:1, 3, 2:3]).then_inc(s_tab, 1)
            dve.wait_ge(s_init, 2)
            ts(le_idle[:, :], c("iota", UNITS)[:, 0:UNITS], idle_upto[:, 0:1], None, ALU.is_ge).then_inc(s_tabv, 1)
            dve.wait_ge(s_tab, 4)
            tt(tab_run[:, :], tab_n[0:1, 1:P + 1], tab_n[0:1, 0:P], ALU.is_equal).then_inc(s_tab, 1)
            dve.wait_ge(s_tabp, 3)
            dve.tensor_copy(tab_idle[:, 0:UNITS], ps[0:1, 4, 0:UNITS]).then_inc(s_tab, 1)
            dve.wait_ge(s_tab, 6)
            n_items = dve.value_load(total[0:1, 0:1], min_val=0, max_val=ITEMS)

            def rstd(root, mv, var, t, done, n1):
                at = ROOT_STEPS * n1
                ts(var[:, :], mv[:, 1:2], EPS, None, ALU.add).then_inc(done, 1)
                dve.wait_ge(done, at + 1)
                ts(t[:, :].bitcast(I32), var[:, :].bitcast(I32), 1, None, ALU.logical_shift_right).then_inc(done, 1)
                dve.wait_ge(done, at + 2)
                ts(root[:, :].bitcast(I32), t[:, :].bitcast(I32), -1.0, float(0x5F3759DF),
                   ALU.mult, ALU.add).then_inc(done, 1)
                for k, three in enumerate((3.0, 12.0, 768.0)):
                    dve.wait_ge(done, at + 3 + 2 * k)
                    ts(t[:, :], root[:, :], root[:, 0:1], var[:, 0:1], ALU.mult, ALU.mult).then_inc(done, 1)
                    dve.wait_ge(done, at + 4 + 2 * k)
                    ts(root[:, :], t[:, :], three, root[:, 0:1], ALU.subtract, ALU.mult).then_inc(done, 1)
                dve.wait_ge(done, at + ROOT_STEPS)

            def norm_x(n1):
                xs = x_sb[:, bass.ds((n1 % 2) * D, D)]
                dve.wait_ge(s_x, 16 * n1)
                dve.bn_stats(x_stats[:, :], xs).then_inc(s_xstat, 1)
                wait_alone(dve, s_xstat, n1)
                dve.bn_aggr(x_mv[:, :], x_stats[:, :]).then_inc(s_xmv, 1)
                dve.wait_ge(s_xmv, n1)
                rstd(x_rstd, x_mv, x_var, x_t, s_xrstd, n1)
                dve.wait_ge(s_xT_ps, n1)
                ts(xn[:, :], xs, x_mv[:, 0:1], x_rstd[:, 0:1], ALU.subtract, ALU.mult).then_inc(s_xn, 1)

            def null_scores(n1):
                dve.wait_ge(s_kv, 3 * (n1 + 1))
                tt(m_st[:, 0:H].rearrange("p (a s k) -> p a s k", s=2, k=HG),
                   null_raw[:, :].rearrange("p (a k s) -> p a s k", s=2, k=HG),
                   nbias_sb[:, :].rearrange("p (a s k) -> p a s k", s=2, k=HG), ALU.add).then_inc(s_m0, 1)

            with dve.If(n_items > 0):
                norm_x(1)
                dve.nop()

            dve.wait_ge(s_small, 7 * 16)
            for k in range(KT):
                dve.wait_ge(s_wqs, k + 1)
                if k > 0:
                    dve.wait_ge(s_wn, k)
                tt(wnull_tmp[:, :].rearrange("p (h d) -> p h d", d=DH), wq_sb[:, k, :].rearrange("p (h d) -> p h d", d=DH),
                   nkey_sb[:, :].unsqueeze(1).to_broadcast([P, H, DH]), ALU.mult).then_inc(s_init, 1)
                dve.wait_ge(s_init, 3 + k)
                dve.tensor_reduce(wvn_sb[:, k, DH:DH + H], wnull_tmp[:, :].rearrange("p (h d) -> p h d", d=DH),
                                  AX.X, ALU.add).then_inc(s_wn, 1)
            dve.tensor_copy(nvcols_sb[:, :], nvcol_sb[:, 0:1].to_broadcast([P, P])).then_inc(s_nvcols, 1)
            dve.tensor_copy(o_st[:, 0:INNER].rearrange("p (h d) -> p h d", d=DH),
                            nval_sb[:, :].unsqueeze(1).to_broadcast([P, H, DH])).then_inc(s_wn, 1)
            dve.wait_ge(s_keepbc, 16)
            ts(maskadd[:, :], keep_bc[:, :], 1.0, -NEG, ALU.subtract, ALU.mult).then_inc(s_maskadd, 1)
            with dve.If(n_items > 0):
                null_scores(1)
                dve.nop()

            dve.wait_ge(s_null_ps, 1)
            dve.bn_stats(y_stats[:, :], ps[:, ps_s[0], :]).then_inc(s_nullv, 1)
            dve.wait_ge(s_nullv, 1)
            dve.bn_aggr(y_mv[:, :], y_stats[:, :]).then_inc(s_nullv, 1)
            dve.wait_ge(s_nullv, 2)
            rstd(y_rstd, y_mv, y_var, y_t, s_nroot, 1)
            ts(null_row[:, :], ps[:, ps_s[0], :], y_mv[:, 0:1], y_rstd[:, 0:1],
               ALU.subtract, ALU.mult).then_inc(s_nullv, 1)
            dve.wait_ge(s_nullv, 3)
            dve.wait_ge(s_prep, 3)
            tt(null_row[:, :], null_row[:, :], gout_sb[:, :], ALU.mult).then_inc(s_null, 1)
            dve.wait_ge(s_wn, KT + 1)
            dve.wait_ge(s_maskadd, 1)

            with dve.Fori(0, ITEMS) as t:
                with dve.If(t < n_items):
                    n, nn = begun(dve, t)
                    ended = row(dve, tab_n, T_ENDED, t + 1, UNITS)
                    loads = row(dve, tab_n, T_LOADS, t + 1, UNITS, 1)
                    off = row(dve, tab, T_OFF, t, 1)
                    kv = row(dve, tab, T_KV, t, UNITS - 1)
                    slot = row(dve, tab, T_SLOT, t, NB - 1)
                    running = row(dve, tab_run, 0, t, 1)
                    a0 = where["tri"][0]
                    dve.wait_ge(s_s_ps, G * (t + 1))
                    tt(mask_cur[:, :], const_sb[:, bass.ds(off * P + a0, P)], maskadd[:, bass.ds(kv * P, P)],
                       ALU.add).then_inc(s_mcur, 1)
                    with dve.If(nn > n):
                        n_next = dve.snap(nn, min_val=2)
                        norm_x(n_next)
                        dve.nop()
                    dve.wait_ge(s_bias, 16 * loads)
                    dve.wait_ge(s_pt_ps, G * (t + 1))
                    for g in range(G):
                        sg = s_sb[:, g * HG:(g + 1) * HG, :]
                        dve.wait_ge(s_s_ps, G * (t + 1) + g + 1)
                        tt(sg.rearrange("p h k -> p (h k)"), ps[:, ps_s[g % 2], :],
                           bias_sb[:, bass.ds(slot * (H * P) + g * GW, GW)], ALU.add).then_inc(s_add, 1)
                        dve.wait_ge(s_add, G * (t + 1) + g + 1)
                        dve.tensor_reduce(m_grp[:, g * HG:(g + 1) * HG], sg, AX.X, ALU.max).then_inc(s_mgrp, 1)
                    m_old = m_st[:, bass.ds(running * H, H)]
                    dve.wait_ge(s_mgrp, G * (t + 1))
                    dve.wait_ge(s_m0, n + 1)
                    tt(m_new[:, :], m_old, m_grp[:, :], ALU.max).then_inc(s_mnew, 1)
                    dve.wait_ge(s_mnew, t + 1)
                    ts(m_neg[:, :], m_new[:, :], -1.0, None, ALU.mult).then_inc(s_mneg, 1)
                    tt(m_drop[:, :], m_old, m_new[:, :], ALU.subtract).then_inc(s_mneg, 1)
                    dve.wait_ge(s_mneg, 2 * (t + 1))
                    dve.tensor_copy(m_st[:, H:2 * H], m_new[:, :])
                    with dve.If(nn > n):
                        n_next = dve.snap(nn, min_val=2)
                        null_scores(n_next)
                        dve.nop()
                    dve.wait_ge(s_alpha, t + 1)
                    tt(o_st[:, INNER:2 * INNER].rearrange("p (h d) -> p h d", d=DH),
                       o_st[:, bass.ds(running * INNER, INNER)].rearrange("p (h d) -> p h d", d=DH),
                       alpha[:, :].unsqueeze(2).to_broadcast([P, H, DH]), ALU.mult).then_inc(s_omul, 1)
                    tt(l_old[:, :], l_st[:, bass.ds(running * H, H)], alpha[:, :], ALU.mult).then_inc(s_lold, 1)
                    for g in range(G):
                        dve.wait_ge(s_pt_ps, G * (t + 1) + g + 1)
                        dve.wait_ge(s_pv, G * (t + 1) + g - 1)
                        dve.tensor_copy(p_T[:, g % 2, :], ps[:, ps_t[g % 2], :]).then_inc(s_pt, 1)
                    dve.wait_ge(s_lold, t + 1)
                    dve.wait_ge(s_p, G * (t + 1))
                    tt(l_st[:, H:2 * H], l_old[:, :], p_sum[:, :], ALU.add).then_inc(s_l, 1)
                    dve.wait_ge(s_omul, t + 1)
                    for a in range(2):
                        o_half = o_st[:, INNER + a * BANK:INNER + (a + 1) * BANK]
                        dve.wait_ge(s_pv, G * (t + 1) + 2 * (a + 1))
                        tt(o_half, o_half, ps[:, ps_q[a], :], ALU.add).then_inc(s_o, 1)
                    with dve.If(ended == n):
                        dve.wait_ge(s_l, t + 1)
                        dve.reciprocal(l_inv[:, :], l_st[:, H:2 * H]).then_inc(s_linv, 1)
                        dve.wait_ge(s_linv, n)
                        dve.wait_ge(s_o, 2 * (t + 2))
                        dve.wait_ge(s_ot_ps, 2 * n)
                        tt(o_n[:, :].rearrange("p (h d) -> p h d", d=DH),
                           o_st[:, INNER:2 * INNER].rearrange("p (h d) -> p h d", d=DH),
                           l_inv[:, :].unsqueeze(2).to_broadcast([P, H, DH]), ALU.mult).then_inc(s_on, 1)
                        dve.wait_ge(s_y_ps, n)
                        dve.bn_stats(y_stats[:, :], ps[:, ps_x, :]).then_inc(s_ystat, 1)
                        wait_alone(dve, s_ystat, n)
                        dve.bn_aggr(y_mv[:, :], y_stats[:, :]).then_inc(s_ymv, 1)
                        dve.wait_ge(s_ymv, n)
                        rstd(y_rstd, y_mv, y_var, y_t, s_yrstd, n)
                        dve.wait_ge(s_yout, 16 * n)
                        ts(y_sb[:, :], ps[:, ps_x, :], y_mv[:, 0:1], y_rstd[:, 0:1],
                           ALU.subtract, ALU.mult).then_inc(s_yread, 1)
                        dve.wait_ge(s_yread, n + 2)
                        tt(y_sb[:, :], y_sb[:, :], gout_sb[:, :], ALU.mult).then_inc(s_yg, 1)
                        dve.wait_ge(s_yg, n)
                        tt(y_sb[:, :], y_sb[:, :], x_sb[:, bass.ds((n % 2) * D, D)], ALU.add).then_inc(s_y, 1)
                        dve.nop()
                    dve.nop()


def head_order():
    return [8 * (g // 2) + 2 * k + g % 2 for g in range(G) for k in range(HG)]


def kernel(**inputs):
    import concourse.bacc as bacc
    from concourse.bass_utils import run_bass_kernel_spmd

    take = {k: np.asarray(v) for k, v in inputs.items()}
    order = head_order()
    fside = take["fside_16xSxS_0"][order]
    fside = fside.reshape(H, NB, P, NB, P).transpose(1, 3, 2, 0, 4).reshape(NB * NB * P, H * P)
    mask = take["mask_BxS_bk0"]
    arrays = {
        "x": take["x"],
        "bias": fside,
        "keep": mask.reshape(UNITS, P),
        "keep_row": mask.reshape(1, UNITS * P),
        "cond": take["cond_64"],
        "g_in": take["L0_cond_g_in"].reshape(KT, P).T,
        "null_bias": take["L0_cond_null_attn_bias"][order].reshape(1, H),
        "wq": take["L0_cond_Wq"],
        "wkv": take["L0_cond_Wkv"],
        "wo": take["L0_cond_Wo"].reshape(H, DH, D)[order].reshape(INNER, D),
        "g_out": take["L0_cond_g_out"].reshape(1, D),
        "const": np.concatenate(list(constants().values()), 1),
    }
    arrays = {k: np.ascontiguousarray(v) for k, v in arrays.items()}
    nc = bacc.Bacc("TRN2", target_bir_lowering=False, num_devices=1)
    args = [nc.dram_tensor(f"{k}_dram", v.shape, mybir.dt.from_np(v.dtype), kind="ExternalInput").ap()
            for k, v in arrays.items()]
    out = nc.dram_tensor("out_dram", (B, S, D), F32, kind="ExternalOutput").ap()
    attention(nc, *args, out)
    r = run_bass_kernel_spmd(nc, [{f"{k}_dram": v for k, v in arrays.items()}], core_ids=[0])
    return r.results[0]["out_dram"]
```
